# Optimizing a Trainium2 kernel written in Bass

```python
import numpy as np
import jax
import jax.numpy as jnp

def _softmax(x, axis=-1):
    return jax.nn.softmax(x, axis=axis)

def _gelu(x):
    return jax.nn.gelu(x, approximate=True)

def _silu(x):
    return jax.nn.silu(x)

def _sigmoid(x):
    return jax.nn.sigmoid(x)

def _layernorm(x, axis=-1, eps=1e-05):
    m = jnp.mean(x, axis=axis, keepdims=True)
    v = jnp.var(x, axis=axis, keepdims=True)
    return (x - m) / jnp.sqrt(v + eps)

def _scatter_add(tgt, idx, src, axis=0):
    return tgt.at[idx].add(src)

def _segment_sum(src, seg, n):
    return jax.ops.segment_sum(src, seg, n)
kernel_name = 'mk_gnn_resnorm_d2_gnn_r64_374269'

def setup_inputs(seed: int=0):
    np.random.seed(seed)
    _w = jnp.asarray

    def _rec_inputs():
        import jax
        import jax.numpy as jnp
        _gk = jax.random.key(seed)
        x = -0.0003713 + 1 * jax.random.normal(jax.random.fold_in(_gk, 1), (100000, 128), jnp.float32)
        src = jax.random.randint(jax.random.fold_in(_gk, 2), (50000,), 0, 100000, jnp.int32)
        dst = jax.random.randint(jax.random.fold_in(_gk, 3), (50000,), 0, 100000, jnp.int32)
        _o = jnp.argsort(dst, stable=True)
        src = src[_o]
        dst = dst[_o]
        return (x, src, dst)
    x, src, dst = _rec_inputs()

    def _L0_gnn_setup():
        import jax, jax.numpy as jnp
        import numpy as np
        N_NODES = 100000

        def _sage_conv(x, src, dst, Wl, bl, Wr):
            msg_sum = jax.ops.segment_sum(x[src], dst, num_segments=N_NODES)
            deg = jax.ops.segment_sum(jnp.ones_like(src, dtype=x.dtype), dst, num_segments=N_NODES)
            mean = msg_sum / jnp.maximum(deg, 1.0)[:, None]
            return mean @ Wl.T + bl + x @ Wr.T
        key = jax.random.key(seed)
        ks = jax.random.split(key, 8)
        in_ch, hid, E = (128, 128, 25000)
        x = jax.random.normal(ks[0], (N_NODES, in_ch), dtype=jnp.float32)
        edge_index = jax.random.randint(ks[1], (2, E), 0, N_NODES, dtype=jnp.int64)
        s1 = 1.0 / np.sqrt(in_ch)
        s2 = 1.0 / np.sqrt(hid)
        W1l = jax.random.uniform(ks[2], (hid, in_ch), jnp.float32, -s1, s1)
        b1l = jax.random.uniform(ks[3], (hid,), jnp.float32, -s1, s1)
        W1r = jax.random.uniform(ks[4], (hid, in_ch), jnp.float32, -s1, s1)
        W2l = jax.random.uniform(ks[5], (hid, hid), jnp.float32, -s2, s2)
        b2l = jax.random.uniform(ks[6], (hid,), jnp.float32, -s2, s2)
        W2r = jax.random.uniform(ks[7], (hid, hid), jnp.float32, -s2, s2)
        return {'x': x, 'edge_index': edge_index, 'W1l': W1l, 'b1l': b1l, 'W1r': W1r, 'W2l': W2l, 'b2l': b2l, 'W2r': W2r}
    _L0_gnn_all = _L0_gnn_setup()
    _L0_gnn_in = {k: v for k, v in _L0_gnn_all.items() if k in ('W1l', 'b1l', 'W1r', 'W2l', 'b2l', 'W2r')}
    del _L0_gnn_all

    def _L1_gnn_setup():
        import jax, jax.numpy as jnp
        import numpy as np
        N_NODES = 50000
        N_EDGES = 12500
        D_IN = 128
        HIDDEN = 256
        OUT = HIDDEN // 2

        def _glorot(key, shape):
            fan_in, fan_out = shape
            lim = jnp.sqrt(6.0 / (fan_in + fan_out))
            return jax.random.uniform(key, shape, jnp.float32, -lim, lim)

        def _sage_conv(x, src, dst, Wl, b, Wr):
            n = x.shape[0]
            agg = jax.ops.segment_sum(x[src], dst, num_segments=n)
            cnt = jax.ops.segment_sum(jnp.ones((src.shape[0],), x.dtype), dst, num_segments=n)
            mean = agg / jnp.maximum(cnt, 1.0)[:, None]
            return mean @ Wl + b + x @ Wr
        key = jax.random.key(seed)
        ks = jax.random.split(key, 11)
        x = jax.random.normal(ks[0], (N_NODES, D_IN), jnp.float32)
        edge_index = jax.random.randint(ks[1], (2, N_EDGES), 0, N_NODES, jnp.int64)
        return {'x': x, 'edge_index': edge_index, 'W1l': _glorot(ks[2], (D_IN, HIDDEN)), 'b1': jnp.zeros((HIDDEN,), jnp.float32), 'W1r': _glorot(ks[3], (D_IN, HIDDEN)), 'W2l': _glorot(ks[4], (HIDDEN, HIDDEN)), 'b2': jnp.zeros((HIDDEN,), jnp.float32), 'W2r': _glorot(ks[5], (HIDDEN, HIDDEN)), 'W3l': _glorot(ks[6], (HIDDEN, OUT)), 'b3': jnp.zeros((OUT,), jnp.float32), 'W3r': _glorot(ks[7], (HIDDEN, OUT))}
    _L1_gnn_all = _L1_gnn_setup()
    _L1_gnn_in = {k: v for k, v in _L1_gnn_all.items() if k in ('W1l', 'b1', 'W1r', 'W2l', 'b2', 'W2r', 'W3l', 'b3', 'W3r')}
    del _L1_gnn_all
    return {'x': x, 'src': src, 'dst': dst, 'L0_gnn_W1l': _L0_gnn_in['W1l'], 'L0_gnn_b1l': _L0_gnn_in['b1l'], 'L0_gnn_W1r': _L0_gnn_in['W1r'], 'L0_gnn_W2l': _L0_gnn_in['W2l'], 'L0_gnn_b2l': _L0_gnn_in['b2l'], 'L0_gnn_W2r': _L0_gnn_in['W2r'], 'L1_gnn_W1l': _L1_gnn_in['W1l'], 'L1_gnn_b1': _L1_gnn_in['b1'], 'L1_gnn_W1r': _L1_gnn_in['W1r'], 'L1_gnn_W2l': _L1_gnn_in['W2l'], 'L1_gnn_b2': _L1_gnn_in['b2'], 'L1_gnn_W2r': _L1_gnn_in['W2r'], 'L1_gnn_W3l': _L1_gnn_in['W3l'], 'L1_gnn_b3': _L1_gnn_in['b3'], 'L1_gnn_W3r': _L1_gnn_in['W3r']}

def reference(x, src, dst, L0_gnn_W1l, L0_gnn_b1l, L0_gnn_W1r, L0_gnn_W2l, L0_gnn_b2l, L0_gnn_W2r, L1_gnn_W1l, L1_gnn_b1, L1_gnn_W1r, L1_gnn_W2l, L1_gnn_b2, L1_gnn_W2r, L1_gnn_W3l, L1_gnn_b3, L1_gnn_W3r):
    import jax
    import jax.numpy as jnp

    def _L0_gnn_ref(x, edge_index, W1l, b1l, W1r, W2l, b2l, W2r):
        import jax, jax.numpy as jnp
        import numpy as np
        N_NODES = 100000

        def _sage_conv(x, src, dst, Wl, bl, Wr):
            msg_sum = jax.ops.segment_sum(x[src], dst, num_segments=N_NODES)
            deg = jax.ops.segment_sum(jnp.ones_like(src, dtype=x.dtype), dst, num_segments=N_NODES)
            mean = msg_sum / jnp.maximum(deg, 1.0)[:, None]
            return mean @ Wl.T + bl + x @ Wr.T
        src, dst = (edge_index[0], edge_index[1])
        h = _sage_conv(x, src, dst, W1l, b1l, W1r)
        h = jax.nn.relu(h)
        h = _sage_conv(h, src, dst, W2l, b2l, W2r)
        return h

    def _L1_gnn_ref(x, edge_index, W1l, b1, W1r, W2l, b2, W2r, W3l, b3, W3r):
        import jax, jax.numpy as jnp
        import numpy as np
        N_NODES = 50000
        N_EDGES = 12500
        D_IN = 128
        HIDDEN = 256
        OUT = HIDDEN // 2

        def _glorot(key, shape):
            fan_in, fan_out = shape
            lim = jnp.sqrt(6.0 / (fan_in + fan_out))
            return jax.random.uniform(key, shape, jnp.float32, -lim, lim)

        def _sage_conv(x, src, dst, Wl, b, Wr):
            n = x.shape[0]
            agg = jax.ops.segment_sum(x[src], dst, num_segments=n)
            cnt = jax.ops.segment_sum(jnp.ones((src.shape[0],), x.dtype), dst, num_segments=n)
            mean = agg / jnp.maximum(cnt, 1.0)[:, None]
            return mean @ Wl + b + x @ Wr
        src, dst = (edge_index[0], edge_index[1])
        h = jax.nn.relu(_sage_conv(x, src, dst, W1l, b1, W1r))
        h = jax.nn.relu(_sage_conv(h, src, dst, W2l, b2, W2r))
        h = _sage_conv(h, src, dst, W3l, b3, W3r)
        return h
    edge_index = jnp.stack([src, dst])
    x = _layernorm(x + _L0_gnn_ref(x, edge_index, L0_gnn_W1l, L0_gnn_b1l, L0_gnn_W1r, L0_gnn_W2l, L0_gnn_b2l, L0_gnn_W2r), axis=-1)
    x = _layernorm(x + _L1_gnn_ref(x, edge_index, L1_gnn_W1l, L1_gnn_b1, L1_gnn_W1r, L1_gnn_W2l, L1_gnn_b2, L1_gnn_W2r, L1_gnn_W3l, L1_gnn_b3, L1_gnn_W3r), axis=-1)
    return x

_drawn_inputs = setup_inputs


def setup_inputs(seed=0):
    import zlib

    import numpy as np

    out = dict(_drawn_inputs(seed))
    spreads = {'L1_gnn_b1': (0.0, 0.1), 'L1_gnn_b2': (0.0, 0.1), 'L1_gnn_b3': (0.0, 0.1)}
    factors = {'L0_gnn_b1l': 2.905}
    for name, (base, spread) in spreads.items():
        noise = np.random.default_rng([zlib.crc32(name.encode()), seed]).standard_normal(out[name].shape)
        drawn = base * np.exp(spread * noise) if base else spread * noise
        out[name] = jnp.asarray(drawn.astype(out[name].dtype))
    for name, factor in factors.items():
        out[name] = (out[name] * factor).astype(out[name].dtype)
    return out
```

```python
from contextlib import ExitStack

import concourse.bass as bass
from concourse import mybir

ALU = mybir.AluOpType
ACT = mybir.ActivationFunctionType
F32 = mybir.dt.float32
F32R = mybir.dt.float32r
I32 = mybir.dt.int32

P = 128
T = 4
GROUP = P * T
EPS = 1e-5
NOWHERE = 1 << 28
RING = 32
LEAD = 6
BEHIND, AHEAD = 12, 5


class Counter:

    def __init__(self, sem, step=1):
        self.sem, self.step, self.base = sem, step, 0

    def at(self, k):
        return k * self.step + self.base

    def passed(self, k):
        self.base += k * self.step


class Program:
    def __init__(self, nc, ctx, n_nodes, n_edges):
        self.nc, self.ctx, self.N, self.E = nc, ctx, n_nodes, n_edges
        self.groups = -(-n_nodes // GROUP)
        self.etiles = -(-n_edges // P)
        self.slots = self.groups * T
        self.block = max(n for n in range(1, P + 1) if self.slots % n == 0)
        self.names = {}
        self.stage = "all"

    def counter(self, name, step=1):
        if name not in self.names:
            self.names[name] = Counter(self.ctx.enter_context(self.nc.semaphore(name)), step)
        return self.names[name]

    def sb(self, ctx, name, shape, dt=F32):
        return ctx.enter_context(self.nc.sbuf_tensor(f"{name}_{self.stage}", shape, dt))

    def ps(self, ctx, name, shape=(P, 512), dt=F32):
        return ctx.enter_context(self.nc.psum_tensor(f"{name}_{self.stage}", list(shape), dt))


def constants(pr):
    nc = pr.nc
    c = pr.ctx
    pr.ident = pr.sb(c, "ident", [P, P])
    pr.ones = pr.sb(c, "ones", [1, P])
    pr.one_col = pr.sb(c, "one_col", [P, 1])
    pr.ones_r = pr.sb(c, "ones_r", [2, P], F32R)
    s_zero, s_ident, s_ones = pr.counter("ident_zeroed"), pr.counter("ident_ready"), pr.counter("ones_ready")
    with nc.Block() as block:
        @block.gpsimd
        def _(pool):
            pool.memset(pr.ident[:, :], 0.0).then_inc(s_zero.sem, 1)
            pool.memset(pr.ones[:, :], 1.0).then_inc(s_ones.sem, 1)
            pool.wait_ge(s_zero.sem, 1)
            pool.affine_select(out=pr.ident[:, :], in_=pr.ident[:, :], compare_op=ALU.not_equal, fill=1.0,
                               base=0, pattern=[[-1, P]], channel_multiplier=1).then_inc(s_ident.sem, 1)
            pool.wait_ge(s_ident.sem, 1)
            pool.wait_ge(s_ones.sem, 1)


def edge_tables(pr, src, dst):
    nc, E = pr.nc, pr.E
    J = pr.etiles
    C = -(-E // P)
    C += -C % 8
    full = E // C
    rest = E - full * C
    rows_full, rest_q = E // P, E % P
    J2 = 2 * pr.groups
    pr.t_src = pr.sb(pr.ctx, "t_src", [P, J2], I32)
    pr.t_out = pr.sb(pr.ctx, "t_out", [P, J2], I32)
    pr.t_dst = pr.sb(pr.ctx, "t_dst", [P, J2])
    pr.t_rec = pr.sb(pr.ctx, "t_rec", [P, J2])
    rec_dram = nc.dram_tensor("rec_scratch", [P * C], F32, kind="Internal").ap()
    assert 2 * pr.groups >= J + 1, "two edge tiles a group, and one to spare"
    src1, dst1 = src, dst
    RB = -(-2 * pr.groups // P)
    rec_view = rec_dram
    pr.dst_rows = pr.sb(pr.ctx, "dst_rows", [P, RB, P])
    with ExitStack() as c:
        d_here = pr.sb(c, "d_here", [P, C], I32)
        d_prev = pr.sb(c, "d_prev", [P, C], I32)
        d_next = pr.sb(c, "d_next", [P, C], I32)
        pos = pr.sb(c, "pos", [P, C])
        flag = pr.sb(c, "flag", [P, C])
        first = pr.sb(c, "first", [P, C])
        last = pr.sb(c, "last", [P, C])
        key = pr.sb(c, "key", [P, C])
        rows = pr.sb(c, "rows", [1, 4 * P])
        carry = pr.sb(c, "carry", [P, 2])
        r_src = pr.sb(c, "r_src", [P, RB, P], I32)
        r_dst = pr.sb(c, "r_dst", [P, RB, P], I32)
        r_srcf = pr.sb(c, "r_srcf", [P, RB, P])
        r_dstf = pr.sb(c, "r_dstf", [P, RB, P])
        r_rec = pr.sb(c, "r_rec", [P, RB, P])
        r_end = pr.sb(c, "r_end", [P, RB, P])
        r_out = pr.sb(c, "r_out", [P, RB, P])
        pt = [pr.ps(c, f"pt{i}") for i in range(4)]
        pc = pr.ps(c, "pc")
        s_fill, s_load, s_pos = pr.counter("tab_filled"), pr.counter("tab_loaded", 16), pr.counter("tab_pos")
        s_rows = pr.counter("dst_rows_kept")
        s_v, s_pe, s_rec = pr.counter("tab_dve"), pr.counter("tab_pe"), pr.counter("tab_rec", 16)
        block = c.enter_context(nc.Block())

        @block.gpsimd
        def _(pool):
            pool.iota(pos[:, :], pattern=[[1, C]], base=0, channel_multiplier=C,
                      allow_small_or_imprecise_dtypes=True).then_inc(s_pos.sem, 1)

        n_loads = []

        @block.sync
        def _(sp):
            sp.wait_ge(s_fill.sem, 5)

            def load(to, frm):
                sp.dma_start(to, frm).then_inc(s_load.sem, 16)
                n_loads.append(1)

            def scan_layout(tile, shift):
                lo = 1 if shift < 0 else 0
                if shift < 0:
                    load(tile[0:1, 1:C], dst1[0:C - 1].rearrange("(a n) -> a n", a=1))
                a, b = lo, full
                load(tile[a:b, :], dst1[a * C + shift:b * C + shift].rearrange("(p n) -> p n", n=C))
                left = rest - max(shift, 0)
                load(tile[full:full + 1, 0:left],
                     dst1[full * C + shift:full * C + shift + left].rearrange("(a n) -> a n", a=1))

            for tile, shift in ((d_here, 0), (d_prev, -1), (d_next, 1)):
                scan_layout(tile, shift)
            for tile, arr in ((r_src, src1), (r_dst, dst1)):
                for b in range(RB):
                    n = min(P, rows_full - b * P)
                    load(tile[0:n, b, :], arr[b * P * P:(b * P + n) * P].rearrange("(p n) -> p n", n=P))
                b, p = rows_full // P, rows_full % P
                load(tile[p:p + 1, b, 0:rest_q], arr[rows_full * P:E].rearrange("(a n) -> a n", a=1))
            sp.wait_ge(s_v.sem, K_REC)
            sp.dma_start(rec_view.rearrange("(p n) -> p n", n=C), key[:, :]).then_inc(s_rec.sem, 16)
            sp.wait_ge(s_rec.sem, 16)
            for b in range(RB):
                n = min(P, J - b * P)
                sp.dma_start(r_rec[0:n, b, :],
                             rec_view[b * P * P:(b * P + n) * P].rearrange("(p n) -> p n", n=P)
                             ).then_inc(s_rec.sem, 16)
        N_LOADS = len(n_loads)

        @block.vector
        def _(v):
            def step(ins, k):
                ins.then_inc(s_v.sem, 1)
                v.wait_ge(s_v.sem, k)
            for tile in (d_here, d_prev, d_next):
                v.memset(tile[:, :], -1).then_inc(s_fill.sem, 1)
            v.memset(r_rec[:, :, :], 0.0)
            v.memset(r_src[:, :, :], 0).then_inc(s_fill.sem, 1)
            v.memset(r_dst[:, :, :], NOWHERE).then_inc(s_fill.sem, 1)
            v.wait_ge(s_load.sem, 16 * N_LOADS)
            v.wait_ge(s_pos.sem, 1)
            step(v.tensor_tensor(flag[:, :], d_here[:, :], d_prev[:, :], ALU.not_equal), 1)
            step(v.tensor_tensor(key[:, :], flag[:, :], pos[:, :], ALU.mult), 2)
            step(v.tensor_tensor_scan(first[:, :], key[:, :], key[:, :], 0.0, ALU.max, ALU.max), 3)
            step(v.tensor_tensor(flag[:, :], d_here[:, :], d_next[:, :], ALU.is_equal), 4)
            step(v.scalar_tensor_tensor(out=key[:, :], in0=flag[:, :], scalar=float(1 << 20),
                                        in1=pos[:, :], op0=ALU.mult, op1=ALU.add), 5)
            step(v.tensor_tensor_scan(last[:, ::-1], key[:, ::-1], key[:, ::-1], float(1 << 22),
                                      ALU.min, ALU.min), 6)
            v.wait_ge(s_pe.sem, 2)
            step(v.tensor_copy(rows[:, 0:2 * P], pc[0:1, 0:2 * P]), 7)
            step(v.tensor_tensor_scan(rows[:, 2 * P:3 * P], rows[:, 0:P], rows[:, 0:P], 0.0,
                                      ALU.max, ALU.max), 8)
            step(v.tensor_tensor_scan(rows[:, 4 * P - 1:3 * P - 1:-1], rows[:, 2 * P - 1:P - 1:-1],
                                      rows[:, 2 * P - 1:P - 1:-1], float(1 << 22), ALU.min, ALU.min), 9)
            step(v.memset(rows[:, 0:2 * P], 0.0), 10)
            step(v.tensor_copy(rows[:, 1:P], rows[:, 2 * P:3 * P - 1]), 11)
            step(v.tensor_scalar(rows[:, P:2 * P], rows[:, P:2 * P], float(1 << 22), None, ALU.add), 12)
            step(v.tensor_copy(rows[:, P:2 * P - 1], rows[:, 3 * P + 1:4 * P]), 13)
            v.wait_ge(s_pe.sem, 4)
            step(v.tensor_copy(carry[:, :], pc[:, 2 * P:2 * P + 2]), 14)
            step(v.tensor_scalar(first[:, :], first[:, :], carry[:, 0:1], None, ALU.max), 15)
            step(v.tensor_scalar(last[:, :], last[:, :], carry[:, 1:2], None, ALU.min), 16)
            step(v.scalar_tensor_tensor(out=flag[:, :], in0=last[:, :], scalar=1.0, in1=first[:, :],
                                        op0=ALU.add, op1=ALU.subtract), 17)
            step(v.tensor_scalar(flag[:, :], flag[:, :], 1.0, None, ALU.max), 18)
            step(v.reciprocal(key[:, :], flag[:, :]), K_REC)
            step(v.tensor_copy(r_srcf[:, :, :], r_src[:, :, :]), 20)
            step(v.tensor_copy(r_dstf[:, :, :], r_dst[:, :, :]), 21)
            step(v.memset(r_end[:, :, :], 0.0), 22)
            step(v.tensor_tensor(r_end[:, :, 0:P - 1], r_dst[:, :, 0:P - 1], r_dst[:, :, 1:P],
                                 ALU.is_equal), 23)
            step(v.scalar_tensor_tensor(out=r_out[:, :, :], in0=r_end[:, :, :], scalar=float(NOWHERE),
                                        in1=r_dstf[:, :, :], op0=ALU.mult, op1=ALU.add), 24)
            v.wait_ge(s_rec.sem, 16 * (1 + RB))
            v.wait_ge(s_pe.sem, 5)
            for n, (table, bank) in enumerate(((pr.t_src, 0), (pr.t_dst, 1), (pr.t_rec, 2), (pr.t_out, 3))):
                step(v.tensor_copy(table[:, :], pt[bank][:, 0:J2]), 25 + n)
            v.tensor_copy(pr.dst_rows[:, :, :], r_dstf[:, :, :]).then_inc(s_rows.sem, 1)

        @block.tensor
        def _(pe):
            pe.wait_ge(s_v.sem, 6)
            pe.matmul(pc[0:1, 0:P], first[:, C - 1:C], pr.ident[:, :], start=True, stop=True).then_inc(s_pe.sem, 1)
            pe.matmul(pc[0:1, P:2 * P], last[:, 0:1], pr.ident[:, :], start=True, stop=True).then_inc(s_pe.sem, 1)
            pe.wait_ge(s_v.sem, 13)
            for n in range(2):
                pe.matmul(pc[:, 2 * P + n:2 * P + n + 1], rows[:, n * P:(n + 1) * P], pr.ones[:, 0:1],
                          start=True, stop=True).then_inc(s_pe.sem, 1)
            pe.wait_ge(s_v.sem, 24)
            pe.wait_ge(s_rec.sem, 16 * (1 + RB))
            for bank, tile in enumerate((r_srcf, r_dstf, r_rec, r_out)):
                for b in range(RB):
                    n = min(P, J2 - b * P)
                    mm = pe.transpose(pt[bank][:, b * P:b * P + n], tile[0:n, b, :], pr.ident[0:n, 0:n])
            mm.then_inc(s_pe.sem, 1)


K_REC = 19


def window_tables(pr):
    nc, J, G, S = pr.nc, pr.etiles, pr.groups, pr.slots
    WB = pr.block
    B = S // WB
    RB = -(-2 * G // P)
    J2 = 2 * G
    moved = G * GROUP - pr.N
    dst_dram = nc.dram_tensor("dst_scratch", [RB * P, P], F32, kind="Internal").ap()
    slot_dram = nc.dram_tensor("slot_scratch", [S, 2], I32, kind="Internal").ap()
    c0 = pr.ctx
    pr.t_win2 = pr.sb(c0, "t_win", [P, 2 * S])
    t_win = pr.t_win2[:, :].rearrange("p (i s) -> p i s", s=2)
    pr.t_slot = pr.sb(c0, "t_slot", [1, 2 * S], I32)
    pr.odd = pr.sb(c0, "odd", [1, 1], I32)
    pr.iota = pr.sb(c0, "iota", [P, P])
    with ExitStack() as c:
        tile = pr.sb(c, "w_tile", [WB, B])
        base = pr.sb(c, "w_base", [WB, B])
        end = pr.sb(c, "w_end", [WB, B])
        tail = pr.sb(c, "w_tail", [WB, B])
        firsts = pr.sb(c, "w_firsts", [WB, J2])
        below = pr.sb(c, "w_below", [WB, J2])
        n_base = pr.sb(c, "w_n_base", [WB, B])
        n_end = pr.sb(c, "w_n_end", [WB, B])
        start = pr.sb(c, "w_start", [WB, B])
        off = pr.sb(c, "w_off", [WB, B])
        bad = pr.sb(c, "w_bad", [WB, 4, B])
        bad_sum = pr.sb(c, "w_bad_sum", [WB, 1])
        at = pr.sb(c, "w_at", [WB, B, 2], I32)
        slot = pr.sb(c, "w_slot", [WB, B, 2], I32)
        got = pr.sb(c, "w_got", [WB, 2 * B, P])
        column = pr.sb(c, "w_column", [WB, 2 * B], I32)
        p_first = pr.ps(c, "p_first")
        p_win = [pr.ps(c, f"p_win{i}") for i in range(4)]
        p_bad = pr.ps(c, "p_bad")
        s_i, s_v, s_pe = pr.counter("win_iota"), pr.counter("win_dve"), pr.counter("win_pe")
        s_d, s_g, s_s = pr.counter("win_dram", 16), pr.counter("win_got", 16), pr.counter("win_slots", 16)
        s_m, s_x = pr.counter("win_slot_mod"), pr.counter("win_banks")
        block = c.enter_context(nc.Block())
        LAST = 16 + 4 * B
        PER = 4

        @block.gpsimd
        def _(pool):
            pool.iota(pr.iota[:, :], pattern=[[1, P]], base=0, channel_multiplier=0,
                      allow_small_or_imprecise_dtypes=True)
            pool.iota(tile[:, :], pattern=[[WB, B]], base=0, channel_multiplier=1,
                      allow_small_or_imprecise_dtypes=True).then_inc(s_i.sem, 1)
            pool.wait_ge(s_v.sem, LAST)
            pool.wait_ge(s_d.sem, 16)
            for n in range(2 * B):
                pool.indirect_dma_start(got[:, n, :], None, dst_dram,
                                        bass.IndirectOffsetOnAxis(ap=column[:, n:n + 1], axis=0),
                                        bounds_check=RB * P - 1, oob_is_err=False).then_inc(s_g.sem, 16)

        @block.sync
        def _(sp):
            sp.dma_start(dst_dram.rearrange("(b p) q -> p b q", p=P), pr.dst_rows[:, :, :]).then_inc(s_d.sem, 16)
            sp.wait_ge(s_m.sem, 2)
            sp.dma_start(slot_dram.rearrange("(b p) s -> p b s", p=WB), slot[:, :, :]).then_inc(s_s.sem, 16)
            sp.wait_ge(s_s.sem, 16)
            sp.dma_start(pr.t_slot[:, :], slot_dram.rearrange("(a i) s -> a (i s)", a=1)).then_inc(s_s.sem, 16)
            sp.wait_ge(s_s.sem, 32)

        @block.tensor
        def _(pe):
            for b in range(RB):
                n = min(P, J2 - b * P)
                mm = pe.matmul(p_first[0:WB, b * P:b * P + n], pr.dst_rows[0:n, b, 0:1].to_broadcast([n, WB]),
                               pr.ident[0:n, 0:n], start=True, stop=True)
            mm.then_inc(s_pe.sem, 1)
            pe.wait_ge(s_v.sem, LAST)
            pe.matmul(p_bad[0:1, 0:1], bad_sum[:, :], pr.one_col[0:WB, :], start=True, stop=True).then_inc(s_pe.sem, 1)
            pe.wait_ge(s_x.sem, 2 * B)
            for n in range(2 * B):
                mm = pe.transpose(p_win[n // PER][:, (n % PER) * WB:(n % PER + 1) * WB], got[:, n, :],
                                  pr.ident[0:WB, 0:WB])
            mm.then_inc(s_pe.sem, 1)

        @block.vector
        def _(v):
            steps = []

            def step(ins):
                steps.append(ins)
                ins.then_inc(s_v.sem, 1)
                v.wait_ge(s_v.sem, len(steps))
            v.memset(pr.one_col[:, :], 1.0)
            v.wait_ge(s_i.sem, 1)
            step(v.tensor_scalar(tail[:, :], tile[:, :], float(S - T), float(-moved), ALU.is_ge, ALU.mult))
            step(v.scalar_tensor_tensor(out=base[:, :], in0=tile[:, :], scalar=float(P), in1=tail[:, :],
                                        op0=ALU.mult, op1=ALU.add))
            step(v.tensor_scalar(end[:, :], base[:, :], float(P), None, ALU.add))
            v.wait_ge(s_pe.sem, 1)
            step(v.tensor_copy(firsts[:, :], p_first[0:WB, 0:J2]))
            for b in range(B):
                for lim, num in ((base, n_base), (end, n_end)):
                    step(v.tensor_scalar(below[:, :], firsts[:, :], lim[:, b:b + 1], None, ALU.is_lt))
                    step(v.tensor_reduce(num[:, b:b + 1], below[:, :], mybir.AxisListType.X, ALU.add))
            step(v.memset(bad[:, :, :], 0.0))
            step(v.tensor_scalar(start[:, :], n_base[:, :], -1.0, 0.0, ALU.add, ALU.max))
            step(v.scalar_tensor_tensor(out=bad[:, 0, :], in0=start[:, :], scalar=2.0, in1=n_end[:, :],
                                        op0=ALU.add, op1=ALU.is_lt))
            step(v.scalar_tensor_tensor(out=off[:, :], in0=tile[:, :], scalar=-0.5, in1=start[:, :],
                                        op0=ALU.mult, op1=ALU.add))
            step(v.tensor_scalar(bad[:, 1, :], off[:, :], float(-BEHIND), None, ALU.is_lt))
            step(v.tensor_scalar(bad[:, 2, :], off[:, :], float(AHEAD), None, ALU.is_gt))
            step(v.tensor_reduce(bad_sum[:, :], bad[:, :, :], mybir.AxisListType.XY, ALU.add))
            step(v.tensor_scalar(start[:, :], start[:, :], float(J2 - 2), None, ALU.min))
            step(v.tensor_copy(at[:, :, 0], start[:, :]))
            step(v.tensor_scalar(at[:, :, 1], start[:, :], 1.0, None, ALU.add))
            step(v.tensor_copy(column[:, :], at[:, :, :].rearrange("p b s -> p (b s)")))
            step(v.memset(tail[:, :], 0.0))
            assert len(steps) == LAST
            for n in range(2):
                v.tensor_scalar(slot[:, :, n], at[:, :, n], RING - 1, None, ALU.bitwise_and).then_inc(s_m.sem, 1)
            v.wait_ge(s_g.sem, 16 * 2 * B)
            for n in range(2 * B):
                v.tensor_scalar(got[:, n, :], got[:, n, :], base[:, n // 2:n // 2 + 1], None,
                                ALU.subtract).then_inc(s_x.sem, 1)
            v.wait_ge(s_pe.sem, 3)
            v.tensor_copy(pr.odd[:, :], p_bad[0:1, 0:1])
            for n in range(2 * B):
                v.tensor_copy(t_win[:, (n // 2) * WB:(n // 2 + 1) * WB, n % 2],
                              p_win[n // PER][:, (n % PER) * WB:(n % PER + 1) * WB])


def weights(pr, convs):
    nc = pr.nc
    for cv in convs:
        n = cv["name"]
        kt, fo = cv["w"], cv["f_out"]
        cv["l32"] = pr.sb(pr.ctx, f"{n}_l32", [P, kt, fo])
        cv["l2"] = pr.sb(pr.ctx, f"{n}_l2", [P, kt, 2, fo], F32R)
        cv["r2"] = pr.sb(pr.ctx, f"{n}_r2", [P, kt, 2, fo], F32R)
        cv["r_hi"], cv["r_lo"] = cv["r2"][:, :, 0, :], cv["r2"][:, :, 1, :]
        cv["bias"] = pr.sb(pr.ctx, f"{n}_bias", [P, fo])
        cv["bias2"] = pr.sb(pr.ctx, f"{n}_bias2", [2, 4, P], F32R)
    with ExitStack() as c:
        raws = pr.sb(c, "w_raw", [P, len(convs), 2, 512])
        brows = pr.sb(c, "b_row", [2, len(convs), 256])
        b_hi = pr.sb(c, "b_hi", [2, P], F32R)
        b_lo = pr.sb(c, "b_lo", [2, P])
        zero = pr.sb(c, "b_zero", [2, 4, P])
        r32 = pr.sb(c, "w_r32", [P, 2, 512])
        pw = [pr.ps(c, f"pw{i}") for i in range(2)]
        pbias = pr.ps(c, "pbias")
        s_in = [pr.counter(f"w_loaded{i}", 16) for i in range(len(convs))]
        s_pe, s_out, s_mid = pr.counter("w_turned"), pr.counter("w_done"), pr.counter("w_mid")
        block = c.enter_context(nc.Block())

        @block.sync
        def _(sp):
            for i, cv in enumerate(convs):
                kt, fo = cv["w"], cv["f_out"]
                raw, brow = raws[:, i, :, :], brows[:, i, :]
                for m, key in enumerate(("Wl", "Wr")):
                    to = raw[:, m, 0:kt * fo].rearrange("p (k n) -> p k n", k=kt)
                    if cv["turned"]:
                        sp.dma_start(raw[:, m, 0:P], cv[key]).then_inc(s_in[i].sem, 16)
                    else:
                        sp.dma_start(to, cv[key].rearrange("(k p) n -> p k n", p=P)).then_inc(s_in[i].sem, 16)
                for n in range(2):
                    sp.dma_start(brow[n:n + 1, 0:fo], cv["b"].rearrange("(a n) -> a n", a=1)).then_inc(s_in[i].sem, 16)

        @block.tensor
        def _(pe):
            for i, cv in enumerate(convs):
                pe.wait_ge(s_in[i].sem, 64)
                raw, brow = raws[:, i, :, :], brows[:, i, :]
                if i:
                    pe.wait_ge(s_out.sem, 2 * i)
                if cv["turned"]:
                    for m in range(2):
                        pe.transpose(pw[m][:, 0:P], raw[:, m, 0:P], pr.ident[:, :])
                pe.matmul(pbias[:, 0:cv["f_out"]], pr.ones[:, :], brow[0:1, 0:cv["f_out"]], start=True,
                          stop=True).then_inc(s_pe.sem, 1)

        @block.vector
        def _(v):
            v.memset(zero[:, :, :], 0.0)
            v.memset(r32[:, :, :], 1.0).then_inc(s_mid.sem, 1)
            v.wait_ge(s_mid.sem, 1)
            v.tensor_copy(pr.ones_r[:, :], r32[0:2, 0, 0:P]).then_inc(s_mid.sem, 1)
            v.wait_ge(s_mid.sem, 2)
            for i, cv in enumerate(convs):
                n = cv["w"] * cv["f_out"]
                v.wait_ge(s_pe.sem, i + 1)
                v.wait_ge(s_in[i].sem, 64)
                raw, brow = raws[:, i, :, :], brows[:, i, :]
                left, right = (pw[0][:, 0:n], pw[1][:, 0:n]) if cv["turned"] else (raw[:, 0, 0:n], raw[:, 1, 0:n])
                kt, fo = cv["w"], cv["f_out"]
                cut = lambda t: t.rearrange("p (k n) -> p k n", k=kt)
                v.tensor_copy(cv["l32"][:, :, :], cut(left))
                v.tensor_copy(cv["bias"][:, :], pbias[:, 0:fo])
                v.tensor_copy(r32[:, 0, 0:n], left)
                v.tensor_copy(r32[:, 1, 0:n], right)
                v.tensor_copy(cv["l2"][:, :, 0, :], cut(left))
                v.tensor_copy(cv["r2"][:, :, 0, :], cut(right))
                v.tensor_copy(b_hi[:, :], brow[:, 0:P])
                v.tensor_copy(cv["bias2"][:, :, :], zero[:, :, :]).then_inc(s_mid.sem, 1)
                v.wait_ge(s_mid.sem, 2 * i + 3)
                for m, w2 in enumerate((cv["l2"], cv["r2"])):
                    v.tensor_tensor(w2[:, :, 1, :], cut(r32[:, m, 0:n]), w2[:, :, 0, :].bitcast(F32), ALU.subtract)
                v.tensor_tensor(b_lo[:, :], brow[:, 0:P], b_hi[:, :].bitcast(F32), ALU.subtract).then_inc(s_mid.sem, 1)
                v.wait_ge(s_mid.sem, 2 * i + 4)
                v.tensor_scalar(b_lo[:, :], b_lo[:, :], pr.ident[0:2, 1:2], None, ALU.mult).then_inc(s_out.sem, 1)
                v.wait_ge(s_out.sem, 2 * i + 1)
                for n in (0, 2):
                    ins = v.scalar_tensor_tensor(out=cv["bias2"][:, n, :], in0=b_hi[:, :].bitcast(F32),
                                                 scalar=pr.ident[0:2, 0:1], in1=b_lo[:, :],
                                                 op0=ALU.mult, op1=ALU.add)
                ins.then_inc(s_out.sem, 1)


def node_base(pr, g):
    return pr.N - GROUP if isinstance(g, int) and g == pr.groups - 1 else g * GROUP


def wait(eng, counter, k):
    if not isinstance(k, int) or k > 0:
        eng.wait_ge(counter.sem, counter.at(k))


def pairs(eng, first, end, body):
    turns = (end - first) // 3
    if turns > 0:
        with eng.Fori(0, turns) as turn:
            for n in range(3):
                body(turn * 3 + (first + n))
    for i in range(first + 3 * turns, end):
        body(i)


def fused_pass(pr, cv):
    nc, G = pr.nc, pr.groups
    kt, fo = cv["w"], cv["f_out"]
    narrow = fo == P
    U, per = 2, 2
    h, out, res = cv["h"], cv["out"], cv.get("res")
    norm = res is not None
    ZERO_OP = ALU.max if cv["relu"] else ALU.add
    FUNC = ACT.Relu if cv["relu"] else ACT.Copy
    with ExitStack() as c:
        rows_in = pr.sb(c, "f_rows_in", [P, 2, T, kt * P])
        t_hi = pr.sb(c, "f_t_hi", [P, 2, kt, GROUP], F32R)
        t_lo = pr.sb(c, "f_t_lo", [P, 2, kt, GROUP], F32R)
        e_full = pr.sb(c, "f_e_full", [P, 2, kt * 2 * P]) if narrow else None
        onehot = pr.sb(c, "f_onehot", [P, 2, 2 * T, P], F32R)
        rows_out = pr.sb(c, "f_rows_out", [P, 2, T, fo])
        part = pr.sb(c, "f_part", [P, 2, T, P]) if narrow else None
        e_idx = pr.sb(c, "f_e_idx", [P, 2, 2], I32)
        e_rows = pr.sb(c, "f_e_rows", [P, 2, 2, kt * P])
        e_hi = pr.sb(c, "f_e_hi", [P, 2, kt, 2 * P], F32R)
        e_lo = pr.sb(c, "f_e_lo", [P, 2, kt, 2 * P], F32R)
        ring = pr.sb(c, "f_ring", [P, RING * 2 * fo], F32R)
        held = pr.sb(c, "f_held", [1, 1])
        if norm:
            res_in = pr.sb(c, "f_res_in", [P, 2, T, P])
            total = pr.sb(c, "f_total", [P, 2, T, P])
            stats = pr.sb(c, "f_stats", [P, 2, T, 6])
            mean_var = pr.sb(c, "f_mean_var", [P, 2, T, 2])
            std = pr.sb(c, "f_std", [P, 2, T])
            rstd = pr.sb(c, "f_rstd", [P, 2, T])
            shift = pr.sb(c, "f_shift", [P, 2, T])
            eps = pr.sb(c, "f_eps", [P, 1])
            held_v = pr.sb(c, "f_held_v", [P, 1])
        turned = [pr.ps(c, f"f_turned{i}") for i in range(2)]
        product = [pr.ps(c, f"f_product{i}") for i in range(4)]
        e_turned = pr.ps(c, "f_e_turned")
        e_product = pr.ps(c, "f_e_product")

        rows_here = [pr.counter(f"f_rows_here{i}", 16) for i in range(2)]
        res_here = [pr.counter(f"f_res_here{i}", 16) for i in range(2)]
        stored = [pr.counter(f"f_stored{i}", 16) for i in range(2)]
        gathered = [pr.counter(f"f_gathered{i}", 32) for i in range(2)]
        names = ("turned", "hi", "lo", "onehot", "product", "copied", "part", "sum", "stats", "meanvar", "std",
                 "rstd", "shift", "normed", "index", "held", "eturned", "ehi", "elo", "eproduct", "ringhi",
                 "ringlo", "eps", "efull")
        (s_turned, s_hi, s_lo, s_onehot, s_product, s_copied, s_part, s_sum, s_stats, s_meanvar, s_std, s_rstd,
         s_shift, s_normed, s_index, s_held, s_eturned, s_ehi, s_elo, s_eproduct, s_ringhi, s_ringlo,
         s_eps, s_efull) = [pr.counter("f_" + x) for x in names]
        s_done, per_group, late = (s_normed, 1, 2) if norm else (s_sum, U, 1)
        block = c.enter_context(nc.Block())

        def steps(eng, step):
            L = LEAD // 2
            for p in range(LEAD):
                step(None, p, p % 2, None, p // 2)
            for g in (0, 1):
                step(g, g + LEAD, g, 0, L)
            def pair(i):
                for s in range(2):
                    step(i * 2 + s, i * 2 + (s + LEAD), s, i, i + L)
            pairs(eng, 1, G // 2 - L - 1, pair)
            for g in (G - LEAD - 2, G - LEAD - 1):
                step(g, g + LEAD, g % 2, g // 2, g // 2 + L)
            for g in range(G - LEAD, G):
                step(g, None, g % 2, g // 2, None)

        def is_last(g):
            return isinstance(g, int) and g == G - 1

        def has(g, back):
            return g is not None and not (isinstance(g, int) and g < back)

        def turned_before(g, p):
            if p is None:
                return G - 1 if g == G - LEAD else None
            return None if isinstance(p, int) and p == 0 else p - 1

        def place(p, a):
            return ((p * 2 + a) % RING) * (2 * fo)

        def view(t, g, width):
            return t[bass.ds(node_base(pr, g), GROUP), 0:width].rearrange("(t p) f -> p t f", p=P)

        @block.sync
        def _(sp):
            def load_rows(g, s):
                wait(sp, s_turned, (g - 1) * kt)
                sp.dma_start(rows_in[:, s, :, :], view(h, g, kt * P)).then_inc(rows_here[s].sem, 16)

            def load_res(g, s):
                wait(sp, s_part, (g - 1) * U)
                sp.dma_start(res_in[:, s, :, :], view(res, g, P)).then_inc(res_here[s].sem, 16)

            def store(g, s):
                wait(sp, s_done, (g + 1) * per_group)
                if is_last(g):
                    wait(sp, stored[1 - s], G // 2)
                sp.dma_start(view(out, g, fo), rows_out[:, s, :, :]).then_inc(stored[s].sem, 16)

            for g in (0, 1):
                load_rows(g, g)
                if norm:
                    load_res(g, g)
            load_rows(2, 0)

            def step(g, s, more):
                if not (isinstance(g, int) and g >= G - 3):
                    load_rows(g + 3, 1 - s)
                if has(g, late):
                    store(g - late, (s - late) % 2)
                if more and norm:
                    load_res(g + 2, s)

            for g in (0, 1):
                step(g, g, True)
            with sp.Fori(1, G // 2 - 2) as i:
                for s in range(2):
                    step(i * 2 + s, s, True)
            for g in range(G - 4, G):
                step(g, g % 2, g < G - 2)
            for g in range(G - late, G):
                store(g, g % 2)
            for s in range(2):
                wait(sp, stored[s], G // 2)

        @block.gpsimd
        def _(pool):
            bound = pool.to_reg(pr.N - 1)

            def mark():
                return pool.tensor_tensor(held[:, :], pr.ones[:, 0:1], pr.ones[:, 0:1], ALU.mult)

            def gather(s):
                for a in range(2):
                    pool.indirect_dma_start(e_rows[:, s, a, :], None, h,
                                            bass.IndirectOffsetOnAxis(ap=e_idx[:, s, a:a + 1], axis=0),
                                            bounds_check=bound, oob_is_err=False).then_inc(gathered[s].sem, 16)

            def refill(p, s):
                wait(pool, s_index, p + 1)
                wait(pool, s_held, p - 1)
                mark().then_inc(s_held.sem, 1)
                gather(s)

            def edges_lo(p, s):
                wait(pool, s_efull, p + 1)
                pool.tensor_tensor(e_lo[:, s, :, :].rearrange("p k n -> p (k n)"), e_full[:, s, :],
                                   e_hi[:, s, :, :].rearrange("p k n -> p (k n)").bitcast(F32),
                                   ALU.subtract).then_inc(s_elo.sem, 1)

            def add_residual(g, s, i, u):
                here = slice(u * per, (u + 1) * per)
                if u == 0:
                    wait(pool, res_here[s], i + 1)
                wait(pool, s_copied, g * U + u + 1)
                pool.tensor_tensor(part[:, s, here, :], part[:, s, here, :], res_in[:, s, here, :],
                                   ALU.add).then_inc(s_part.sem, 1)

            def step(g, p, s, i, j):
                if norm and has(g, 1):
                    add_residual(g - 1, 1 - s, i - 1 + s, 1)
                if p is not None and not (isinstance(p, int) and p + 2 >= G):
                    refill(p + 2, s)
                if norm and g is not None:
                    add_residual(g, s, i, 0)
                if narrow and p is not None:
                    edges_lo(p, s)

            mark().then_inc(s_held.sem, 1)
            for p in range(2):
                wait(pool, s_index, p + 1)
                gather(p)
            steps(pool, step)
            if norm:
                add_residual(G - 1, 1, G // 2 - 1, 1)

        @block.tensor
        def _(pe):
            def turn_edges(p, s, j):
                wait(pe, gathered[s], j + 1)
                wait(pe, s_efull if narrow else s_elo, p)
                for k in range(kt):
                    for a in range(2):
                        at = (k * 2 + a) * P
                        mm = pe.transpose(e_turned[:, at:at + P], e_rows[:, s, a, k * P:(k + 1) * P], pr.ident[:, :])
                mm.then_inc(s_eturned.sem, 1)

            def turn_nodes(g, s, i):
                wait(pe, rows_here[s], i + 1)
                for k in range(kt):
                    wait(pe, s_lo, g * kt + k - 1)
                    bank = turned[(s * kt + k) % 2]
                    for t in range(T):
                        mm = pe.transpose(bank[:, t * P:(t + 1) * P], rows_in[:, s, t, k * P:(k + 1) * P],
                                          pr.ident[:, :])
                    mm.then_inc(s_turned.sem, 1)

            def places(g):
                _, at = nc.values_load_multi_w_load_instructions(
                    pr.t_slot[0:1, bass.ds(g * (2 * T), 2 * T)], engines=[mybir.EngineType.PE], min_val=0,
                    max_val=RING - 1, skip_runtime_bounds_check_because="they are numbers modulo RING")
                return at

            def multiply(g, s, at, banks):
                for u in banks:
                    wait(pe, s_onehot, g * U + u + 1)
                    if u == 0:
                        ready = g + LEAD - 2
                        wait(pe, s_lo, (g + 1) * kt)
                        wait(pe, s_ringlo, min(ready, G) if isinstance(g, int) else ready)
                    wait(pe, s_sum, g * U + u - 3)
                    bank = product[s * U + u]
                    if narrow:
                        pe.matmul(bank[:, :], pr.ones_r[:, :], cv["bias2"][:, :, :].rearrange("p a n -> p (a n)"),
                                  start=True, stop=False, skip_group_check=True)
                    for t in range(u * per, (u + 1) * per):
                        to = bank[:, (t % per) * 256:(t % per) * 256 + 256]
                        cols = slice(t * P, (t + 1) * P)
                        for k in range(kt):
                            first = not narrow and k == 0
                            both = cv["r2"][:, k, :, :].rearrange("p a n -> p (a n)")
                            if narrow:
                                pe.matmul(to, t_hi[:, s, k, cols], both, start=False, stop=False,
                                          skip_group_check=True)
                            else:
                                pe.matmul(to, t_hi[:, s, k, cols], cv["r2"][:, k, 0, :], start=first, stop=False)
                                pe.matmul(to, t_hi[:, s, k, cols], cv["r2"][:, k, 1, :], start=False, stop=False)
                            pe.matmul(to[:, 0:fo], t_lo[:, s, k, cols], cv["r2"][:, k, 0, :], start=False,
                                      stop=False, skip_group_check=narrow)
                        for w in range(2):
                            n = 2 * t + w
                            for half in range(1 if narrow else 2):
                                mm = pe.matmul(to, onehot[:, s, n, :],
                                               ring[:, bass.ds(at[n] * (2 * fo) + half * fo, 256)], start=False,
                                               stop=(w == 1 and (narrow or half == 1)), skip_group_check=narrow)
                    mm.then_inc(s_product.sem, 1)

            def project(p, s):
                wait(pe, s_elo, p + 1)
                wait(pe, s_ringlo, p)
                for a in range(2):
                    to = e_product[:, a * fo:(a + 1) * fo]
                    cols = slice(a * P, (a + 1) * P)
                    for k in range(kt):
                        pe.matmul(to, e_hi[:, s, k, cols], cv["l2"][:, k, 0, :], start=(k == 0), stop=False)
                        pe.matmul(to, e_hi[:, s, k, cols], cv["l2"][:, k, 1, :], start=False, stop=False)
                        mm = pe.matmul(to, e_lo[:, s, k, cols], cv["l2"][:, k, 0, :], start=False,
                                       stop=(k == kt - 1))
                mm.then_inc(s_eproduct.sem, 1)

            def step(g, p, s, i, j):
                if g is None and p == LEAD - 1:
                    turn_nodes(0, 0, 0)
                if g is not None:
                    at = places(g)
                    if not is_last(g):
                        turn_nodes(g + 1, 1 - s, i + s)
                    multiply(g, s, at, [0])
                q = turned_before(g, p)
                if q is not None:
                    project(q, 1 - s)
                if p is not None and not (isinstance(p, int) and p == G - 1):
                    turn_edges(p + 1, 1 - s, j + s)
                if g is not None:
                    multiply(g, s, at, [1])
            turn_edges(0, 0, 0)
            steps(pe, step)

        @block.scalar
        def _(act):
            def take_numbers(p, s):
                act.activation(e_idx[:, s, :], pr.t_src[:, bass.ds(p * 2, 2)], ACT.Copy).then_inc(s_index.sem, 1)

            def edges_hi(p, s):
                wait(act, s_eturned, p + 1)
                wait(act, s_eproduct, p - 1)
                act.activation(e_hi[:, s, :, :].rearrange("p k n -> p (k n)"), e_turned[:, 0:kt * 2 * P],
                               FUNC).then_inc(s_ehi.sem, 1)
                if narrow:
                    wait(act, s_elo, p - 1)
                    act.activation(e_full[:, s, :], e_turned[:, 0:kt * 2 * P], FUNC).then_inc(s_efull.sem, 1)

            def nodes_hi(g, s):
                for k in range(kt):
                    wait(act, s_turned, g * kt + k + 1)
                    if k == 0:
                        wait(act, s_product, (g - 1) * U)
                    act.activation(t_hi[:, s, k, :], turned[(s * kt + k) % 2][:, :], FUNC).then_inc(s_hi.sem, 1)

            def copy_half(g, s, u):
                wait(act, s_product, g * U + u + 1)
                wait(act, s_sum, (g - 2) * U + u + 1)
                frm = product[s * U + u][:, :].rearrange("p (t a n) -> p t a n", t=per, a=2)[:, :, 0, :]
                act.activation(part[:, s, u * per:(u + 1) * per, :], frm, ACT.Copy).then_inc(s_copied.sem, 1)

            def ring_hi(p, s):
                wait(act, s_eproduct, p + 1)
                for a in range(2):
                    ins = act.activation(ring[:, bass.ds(place(p, a), fo)], e_product[:, a * fo:(a + 1) * fo],
                                         ACT.Copy, scale=pr.t_rec[:, bass.ds(p * 2 + a, 1)])
                ins.then_inc(s_ringhi.sem, 1)

            def deviation(g, s):
                wait(act, s_meanvar, g + 1)
                act.activation(std[:, s, :], mean_var[:, s, :, 1], ACT.Sqrt, bias=eps[:, :]).then_inc(s_std.sem, 1)

            def normalise(g, s, i):
                wait(act, s_shift, g + 1)
                wait(act, stored[s], i)
                for t in range(T):
                    ins = act.activation(rows_out[:, s, t, :], total[:, s, t, :], ACT.Identity,
                                         scale=rstd[:, s, t:t + 1], bias=shift[:, s, t:t + 1])
                ins.then_inc(s_normed.sem, 1)

            def step(g, p, s, i, j):
                if p is not None:
                    edges_hi(p, s)
                    if not (isinstance(p, int) and p + 2 >= G):
                        take_numbers(p + 2, s)
                if g is None and p == LEAD - 1:
                    nodes_hi(0, 0)
                if narrow and has(g, 1):
                    copy_half(g - 1, 1 - s, 1)
                if g is not None and not is_last(g):
                    nodes_hi(g + 1, 1 - s)
                if norm and has(g, 2):
                    normalise(g - 2, s, i - 1)
                if narrow and g is not None:
                    copy_half(g, s, 0)
                q = turned_before(g, p)
                if q is not None:
                    ring_hi(q, 1 - s)
                if norm and has(g, 1):
                    deviation(g - 1, 1 - s)

            if norm:
                wait(act, s_eps, 1)
            for p in range(2):
                take_numbers(p, p)
            steps(act, step)
            if narrow:
                copy_half(G - 1, 1, 1)
            if norm:
                normalise(G - 2, 0, G // 2 - 1)
                deviation(G - 1, 1)
                normalise(G - 1, 1, G // 2 - 1)

        @block.vector
        def _(v):
            def edges_lo(p, s):
                wait(v, s_ehi, p + 1)
                v.scalar_tensor_tensor(out=e_lo[:, s, :, :].rearrange("p k n -> p (k n)"),
                                       in0=e_turned[:, 0:kt * 2 * P], scalar=0.0,
                                       in1=e_hi[:, s, :, :].rearrange("p k n -> p (k n)").bitcast(F32),
                                       op0=ZERO_OP, op1=ALU.subtract).then_inc(s_elo.sem, 1)

            def nodes_lo(g, s):
                for k in range(kt):
                    wait(v, s_hi, g * kt + k + 1)
                    v.scalar_tensor_tensor(out=t_lo[:, s, k, :], in0=turned[(s * kt + k) % 2][:, :], scalar=0.0,
                                           in1=t_hi[:, s, k, :].bitcast(F32), op0=ZERO_OP,
                                           op1=ALU.subtract).then_inc(s_lo.sem, 1)

            def compare(g, s, u):
                n0, n = u * T, T
                wait(v, s_product, (g - 2) * U + u + 1)
                v.tensor_tensor(onehot[:, s, n0:n0 + n, :], pr.iota[:, :].unsqueeze(1).to_broadcast([P, n, P]),
                                pr.t_win2[:, bass.ds(g * (2 * T) + n0, n)].unsqueeze(2).to_broadcast([P, n, P]),
                                ALU.is_equal).then_inc(s_onehot.sem, 1)

            def add_up(g, s, i, u):
                n = g * U + u
                here = slice(u * per, (u + 1) * per)
                rows = total if norm else rows_out
                if u == 0 and norm:
                    wait(v, s_normed, g - 1)
                elif u == 0:
                    wait(v, stored[s], i)
                if narrow:
                    wait(v, s_part if norm else s_copied, n + 1)
                    halves = product[s * U + u][:, :].rearrange("p (t a n) -> p t a n", t=per, a=2)
                    v.tensor_tensor(rows[:, s, here, :], halves[:, :, 1, :], part[:, s, here, :],
                                    ALU.add).then_inc(s_sum.sem, 1)
                else:
                    wait(v, s_product, n + 1)
                    frm = product[s * U + u][:, :].rearrange("p (t f) -> p t f", f=fo)
                    v.tensor_tensor(rows[:, s, here, :], frm, cv["bias"][:, :].unsqueeze(1).to_broadcast([P, per, fo]),
                                    ALU.add).then_inc(s_sum.sem, 1)

            def moments(g, s):
                wait(v, s_sum, (g + 1) * U)
                for t in range(T):
                    ins = v.bn_stats(stats[:, s, t, :], total[:, s, t, :])
                ins.then_inc(s_stats.sem, 1)

            def aggregate(g, s):
                wait(v, s_stats, g + 1)
                v.memset(held_v[:, :], 0.0)
                for t in range(T):
                    ins = v.bn_aggr(mean_var[:, s, t, :], stats[:, s, t, :])
                ins.then_inc(s_meanvar.sem, 1)

            def inverse(g, s):
                wait(v, s_std, g + 1)
                v.reciprocal(rstd[:, s, :], std[:, s, :]).then_inc(s_rstd.sem, 1)

            def offset(g, s):
                wait(v, s_rstd, g + 1)
                v.scalar_tensor_tensor(out=shift[:, s, :], in0=mean_var[:, s, :, 0], scalar=-1.0,
                                       in1=rstd[:, s, :], op0=ALU.mult, op1=ALU.mult).then_inc(s_shift.sem, 1)

            def ring_lo(p, s):
                wait(v, s_ringhi, p + 1)
                for a in range(2):
                    ins = v.scalar_tensor_tensor(out=ring[:, bass.ds(place(p, a) + fo, fo)],
                                                 in0=e_product[:, a * fo:(a + 1) * fo],
                                                 scalar=pr.t_rec[:, bass.ds(p * 2 + a, 1)],
                                                 in1=ring[:, bass.ds(place(p, a), fo)].bitcast(F32),
                                                 op0=ALU.mult, op1=ALU.subtract)
                ins.then_inc(s_ringlo.sem, 1)

            def step(g, p, s, i, j):
                if norm and g is not None and not is_last(g):
                    compare(g + 1, 1 - s, 0)
                if norm and has(g, 2):
                    inverse(g - 2, s)
                if p is not None and not narrow:
                    edges_lo(p, s)
                if norm and has(g, 2):
                    offset(g - 2, s)
                if g is None:
                    if p == LEAD - 1:
                        nodes_lo(0, 0)
                        compare(0, 0, 0)
                        compare(0, 0, 1)
                    if p > 0:
                        ring_lo(p - 1, 1 - s)
                    return
                if not is_last(g):
                    nodes_lo(g + 1, 1 - s)
                if has(g, 1):
                    add_up(g - 1, 1 - s, i - 1 + s, 1)
                if not norm and not is_last(g):
                    compare(g + 1, 1 - s, 0)
                if not is_last(g):
                    compare(g + 1, 1 - s, 1)
                if norm and has(g, 1):
                    moments(g - 1, 1 - s)
                if norm and has(g, 1):
                    aggregate(g - 1, 1 - s)
                if not norm:
                    add_up(g, s, i, 0)
                q = turned_before(g, p)
                if q is not None:
                    ring_lo(q, 1 - s)
                if norm:
                    add_up(g, s, i, 0)

            if norm:
                v.memset(eps[:, :], EPS).then_inc(s_eps.sem, 1)
            steps(v, step)
            if norm:
                inverse(G - 2, 0)
                offset(G - 2, 0)
            add_up(G - 1, 1, G // 2 - 1, 1)
            if norm:
                moments(G - 1, 1)
                aggregate(G - 1, 1)
                inverse(G - 1, 1)
                offset(G - 1, 1)

    for s in range(2):
        rows_here[s].passed(G // 2)
        stored[s].passed(G // 2)
        gathered[s].passed(G // 2)
        if norm:
            res_here[s].passed(G // 2)
    for q in (s_turned, s_hi, s_lo):
        q.passed(G * kt)
    for q in (s_product, s_sum, s_onehot):
        q.passed(G * U)
    for q in (s_index, s_eturned, s_ehi, s_elo, s_eproduct, s_ringhi, s_ringlo):
        q.passed(G)
    s_held.passed(G - 1)
    if narrow:
        s_copied.passed(G * U)
        s_efull.passed(G)
    if norm:
        s_part.passed(G * U)
        s_eps.passed(1)
        for q in (s_stats, s_meanvar, s_std, s_rstd, s_shift, s_normed):
            q.passed(G)


def dense_pass(pr, cv):
    nc, G = pr.nc, pr.groups
    kt, fo = cv["w"], cv["f_out"]
    U = fo // P
    per = T // U
    h, out, res, relu = cv["h"], cv["out"], cv.get("res"), cv["relu"]
    with ExitStack() as c:
        rows_in = pr.sb(c, "rows_in", [P, 2, T, kt * P])
        res_in = pr.sb(c, "res_in", [P, 2, T, fo]) if res is not None else None
        t_hi = pr.sb(c, "t_hi", [P, 2, kt, GROUP], F32R)
        t_lo = pr.sb(c, "t_lo", [P, 2, kt, GROUP], F32R)
        rows_out = pr.sb(c, "rows_out", [P, 2, T, fo])
        turned = [pr.ps(c, f"turned{i}") for i in range(2)]
        product = [pr.ps(c, f"product{i}") for i in range(4)]
        s_in = [pr.counter(f"rows_in{i}", 16) for i in range(2)]
        s_res = [pr.counter(f"res_in{i}", 16) for i in range(2)]
        s_t, s_hi, s_lo = pr.counter("turned_ready"), pr.counter("hi_ready"), pr.counter("lo_ready")
        s_mm, s_sum, s_out = pr.counter("product_ready"), pr.counter("biased"), pr.counter("rows_ready")
        s_st = [pr.counter(f"stored{i}", 16) for i in range(2)]
        block = c.enter_context(nc.Block())

        def each(eng, body):
            body(0, 0, True)
            body(1, 1, True)
            with eng.Fori(1, G // 2 - 1) as i:
                body(i * 2, 0, False)
                body(i * 2 + 1, 1, False)
            body(G - 2, 0, False)
            body(G - 1, 1, False)

        def view(t, g, width):
            n0 = node_base(pr, g)
            return t[bass.ds(n0, GROUP), 0:width].rearrange("(t p) f -> p t f", p=P)

        def half(g):
            return g // 2 if isinstance(g, int) else g // 2

        @block.sync
        def _(sp):
            def load(g, s, first):
                if not first:
                    sp.wait_ge(s_t.sem, s_t.at((g - 1) * kt))
                sp.dma_start(rows_in[:, s, :, :], view(h, g, kt * P)).then_inc(s_in[s].sem, 16)
                if res is not None:
                    if not first:
                        sp.wait_ge(s_out.sem, s_out.at((g - 1) * U))
                    sp.dma_start(res_in[:, s, :, :], view(res, g, fo)).then_inc(s_res[s].sem, 16)

            def store(g, s):
                sp.wait_ge(s_out.sem, s_out.at((g + 1) * U))
                if isinstance(g, int) and g == G - 1:
                    sp.wait_ge(s_st[1 - s].sem, s_st[1 - s].at(G // 2))
                sp.dma_start(view(out, g, fo), rows_out[:, s, :, :]).then_inc(s_st[s].sem, 16)

            load(0, 0, True)
            load(1, 1, True)
            with sp.Fori(0, G // 2 - 2) as i:
                for s in range(2):
                    store(i * 2 + s, s)
                    load(i * 2 + s + 2, s, False)
            for g in range(G - 4, G - 2):
                store(g, g % 2)
                load(g + 2, g % 2, False)
            store(G - 2, 0)
            store(G - 1, 1)
            for s in range(2):
                sp.wait_ge(s_st[s].sem, s_st[s].at(G // 2))

        def count2(g):
            return g // 2

        @block.tensor
        def _(pe):
            def transposes(g, i, s):
                pe.wait_ge(s_in[s].sem, s_in[s].at(i + 1))
                for k in range(kt):
                    n = g * kt + k
                    bank = (s * kt + k) % 2
                    if not (isinstance(g, int) and n < 2):
                        pe.wait_ge(s_lo.sem, s_lo.at(n - 1))
                    for t in range(T):
                        mm = pe.transpose(turned[bank][:, t * P:(t + 1) * P],
                                          rows_in[:, s, t, k * P:(k + 1) * P], pr.ident[:, :])
                    mm.then_inc(s_t.sem, 1)

            def products(g, i, s):
                pe.wait_ge(s_lo.sem, s_lo.at((g + 1) * kt))
                for u in range(U):
                    n = g * U + u
                    bank = product[(s * U + u) % 4]
                    if not (isinstance(g, int) and g * U + u < 2 * U):
                        pe.wait_ge(s_out.sem, s_out.at(n - 2 * U + 1))
                    for tt in range(per):
                        t = u * per + tt
                        to = bank[:, tt * fo:(tt + 1) * fo]
                        cols = slice(t * P, (t + 1) * P)
                        for k in range(kt):
                            pe.matmul(to, t_hi[:, s, k, cols], cv["r_hi"][:, k, :], start=(k == 0), stop=False)
                            pe.matmul(to, t_hi[:, s, k, cols], cv["r_lo"][:, k, :], start=False, stop=False)
                            mm = pe.matmul(to, t_lo[:, s, k, cols], cv["r_hi"][:, k, :], start=False,
                                           stop=(k == kt - 1))
                    mm.then_inc(s_mm.sem, 1)

            transposes(0, 0, 0)

            def both(g, i, s, more):
                if more:
                    transposes(g + 1, i + s, 1 - s)
                products(g, i, s)
            both(0, 0, 0, True)
            both(1, 0, 1, True)
            with pe.Fori(1, G // 2 - 1) as i:
                both(i * 2, i, 0, True)
                both(i * 2 + 1, i, 1, True)
            both(G - 2, G // 2 - 1, 0, True)
            both(G - 1, G // 2 - 1, 1, False)

        @block.scalar
        def _(act):
            def body(g, s, first):
                for k in range(kt):
                    n = g * kt + k
                    act.wait_ge(s_t.sem, s_t.at(n + 1))
                    if not first and k == 0:
                        act.wait_ge(s_mm.sem, s_mm.at((g - 1) * U))
                    act.activation(t_hi[:, s, k, :], turned[(s * kt + k) % 2][:, :],
                                   ACT.Relu if relu else ACT.Copy).then_inc(s_hi.sem, 1)
            each(act, body)

        @block.vector
        def _(v):
            def halves(g, s):
                for k in range(kt):
                    n = g * kt + k
                    v.wait_ge(s_hi.sem, s_hi.at(n + 1))
                    v.scalar_tensor_tensor(out=t_lo[:, s, k, :], in0=turned[(s * kt + k) % 2][:, :],
                                           scalar=0.0, in1=t_hi[:, s, k, :].bitcast(F32),
                                           op0=ALU.max if relu else ALU.add,
                                           op1=ALU.subtract).then_inc(s_lo.sem, 1)

            def sums(g, i, s, first):
                for u in range(U):
                    n = g * U + u
                    v.wait_ge(s_mm.sem, s_mm.at(n + 1))
                    if u == 0 and not first:
                        v.wait_ge(s_st[s].sem, s_st[s].at(i))
                    to = rows_out[:, s, u * per:(u + 1) * per, :]
                    frm = product[(s * U + u) % 4][:, :].rearrange("p (t f) -> p t f", f=fo)
                    bias = cv["bias"][:, :].unsqueeze(1).to_broadcast([P, per, fo])
                    if res is None:
                        v.tensor_tensor(to, frm, bias, ALU.add).then_inc(s_out.sem, 1)
                    else:
                        v.tensor_tensor(to, frm, bias, ALU.add).then_inc(s_sum.sem, 1)
                        v.wait_ge(s_sum.sem, s_sum.at(n + 1))
                        v.wait_ge(s_res[s].sem, s_res[s].at(i + 1))
                        v.tensor_tensor(to, to, res_in[:, s, u * per:(u + 1) * per, :],
                                        ALU.add).then_inc(s_out.sem, 1)

            halves(0, 0)
            halves(1, 1)
            sums(0, 0, 0, True)
            halves(2, 0)
            sums(1, 0, 1, True)
            with v.Fori(1, G // 2 - 1) as i:
                halves(i * 2 + 1, 1)
                sums(i * 2, i, 0, False)
                halves(i * 2 + 2, 0)
                sums(i * 2 + 1, i, 1, False)
            halves(G - 1, 1)
            sums(G - 2, G // 2 - 1, 0, False)
            sums(G - 1, G // 2 - 1, 1, False)

    for s in range(2):
        s_in[s].passed(G // 2)
        s_st[s].passed(G // 2)
        if res is not None:
            s_res[s].passed(G // 2)
    for q in (s_t, s_hi, s_lo):
        q.passed(G * kt)
    for q in (s_mm, s_out) + ((s_sum,) if res is not None else ()):
        q.passed(G * U)


def edge_pass(pr, cv):
    nc, J = pr.nc, pr.etiles
    kt, fo = cv["w"], cv["f_out"]
    h, out, relu = cv["h"], cv["out"], cv["relu"]
    with ExitStack() as c:
        i_src = pr.sb(c, "i_src", [P, 1], I32)
        i_out = pr.sb(c, "i_out", [P, 1], I32)
        dcol = pr.sb(c, "dcol", [P, 1])
        rcol = pr.sb(c, "rcol", [P, 1])
        rows = pr.sb(c, "e_rows", [P, kt * P])
        scaled = pr.sb(c, "e_scaled", [P, kt * P])
        same = pr.sb(c, "e_same", [P, P])
        sums = pr.sb(c, "e_sums", [P, kt, P])
        proj = pr.sb(c, "e_proj", [P, fo])
        held = pr.sb(c, "e_held", [1, 1])
        p_dst = pr.ps(c, "p_dst")
        p_sum = pr.ps(c, "p_sum")
        p_out = pr.ps(c, "p_out")
        s_idx, s_got, s_add = pr.counter("e_idx"), pr.counter("e_gathered", 16), pr.counter("e_added", 16)
        s_v, s_pe, s_held = pr.counter("e_dve"), pr.counter("e_pe"), pr.counter("e_held")
        block = c.enter_context(nc.Block())

        @block.gpsimd
        def _(pool):
            def carrier(n):
                pool.wait_ge(s_held.sem, s_held.at(n))
                pool.tensor_tensor(held[:, :], pr.ones[:, 0:1], pr.ones[:, 0:1], ALU.mult).then_inc(s_held.sem, 1)

            bound = pool.to_reg(pr.N - 1)
            pool.tensor_tensor(held[:, :], pr.ones[:, 0:1], pr.ones[:, 0:1], ALU.mult).then_inc(s_held.sem, 1)

            def gather():
                pool.indirect_dma_start(rows[:, :], None, h, bass.IndirectOffsetOnAxis(ap=i_src[:, :], axis=0),
                                        bounds_check=bound, oob_is_err=False).then_inc(s_got.sem, 16)

            def add():
                pool.indirect_dma_start(out, bass.IndirectOffsetOnAxis(ap=i_out[:, :], axis=0), proj[:, :], None,
                                        bounds_check=bound, oob_is_err=False,
                                        compute_op=ALU.add).then_inc(s_add.sem, 16)

            pool.wait_ge(s_idx.sem, s_idx.at(1))
            gather()
            pool.wait_ge(s_v.sem, s_v.at(4))
            add()
            with pool.Fori(1, J) as j:
                pool.wait_ge(s_idx.sem, s_idx.at(j + 1))
                carrier(2 * j - 1)
                gather()
                pool.wait_ge(s_v.sem, s_v.at(4 * j + 4))
                pool.wait_ge(s_add.sem, s_add.at(j))
                carrier(2 * j)
                add()
            pool.wait_ge(s_add.sem, s_add.at(J))

        @block.vector
        def _(v):
            def tile(j, first):
                col = bass.ds(j, 1)
                if not first:
                    v.wait_ge(s_add.sem, s_add.at(j))
                v.tensor_copy(i_src[:, :], pr.t_src[:, col])
                v.tensor_copy(rcol[:, :], pr.t_rec[:, col])
                v.tensor_copy(dcol[:, :], pr.t_dst[:, col])
                v.tensor_copy(i_out[:, :], pr.t_out[:, col]).then_inc(s_idx.sem, 1)
                v.wait_ge(s_idx.sem, s_idx.at(j + 1))
                v.wait_ge(s_got.sem, s_got.at(j + 1))
                v.tensor_scalar(scaled[:, :], rows[:, :], rcol[:, :], 0.0 if relu else None, ALU.mult,
                                ALU.max if relu else ALU.bypass).then_inc(s_v.sem, 1)
                v.wait_ge(s_pe.sem, s_pe.at(3 * j + 1))
                v.tensor_scalar(same[:, :], p_dst[:, 0:P], dcol[:, :], None, ALU.is_equal).then_inc(s_v.sem, 1)
                v.wait_ge(s_pe.sem, s_pe.at(3 * j + 2))
                v.tensor_copy(sums[:, :, :].rearrange("p k n -> p (k n)"), p_sum[:, 0:kt * P]).then_inc(s_v.sem, 1)
                v.wait_ge(s_pe.sem, s_pe.at(3 * j + 3))
                v.tensor_copy(proj[:, :], p_out[:, 0:fo]).then_inc(s_v.sem, 1)
            tile(0, True)
            with v.Fori(1, J) as j:
                tile(j, False)

        @block.tensor
        def _(pe):
            with pe.Fori(0, J) as j:
                pe.wait_ge(s_idx.sem, s_idx.at(j + 1))
                pe.matmul(p_dst[:, 0:P], dcol[:, :].to_broadcast([P, P]), pr.ident[:, :], start=True,
                          stop=True).then_inc(s_pe.sem, 1)
                pe.wait_ge(s_v.sem, s_v.at(4 * j + 2))
                for k in range(kt):
                    mm = pe.matmul(p_sum[:, k * P:(k + 1) * P], scaled[:, k * P:(k + 1) * P], same[:, :],
                                   start=True, stop=True)
                mm.then_inc(s_pe.sem, 1)
                pe.wait_ge(s_v.sem, s_v.at(4 * j + 3))
                for k in range(kt):
                    mm = pe.matmul(p_out[:, 0:fo], sums[:, k, :], cv["l32"][:, k, :], start=(k == 0),
                                   stop=(k == kt - 1))
                mm.then_inc(s_pe.sem, 1)

    s_idx.passed(J)
    s_held.passed(2 * J - 1)
    s_got.passed(J)
    s_add.passed(J)
    s_v.passed(4 * J)
    s_pe.passed(3 * J)


def norm_pass(pr, frm, to):
    nc, G = pr.nc, pr.groups
    with ExitStack() as c:
        rows = pr.sb(c, "n_rows", [P, 2, T, P])
        done = pr.sb(c, "n_done", [P, 2, T, P])
        stats = pr.sb(c, "n_stats", [P, 2, T, 6])
        mv = pr.sb(c, "n_mv", [P, 2, T, 2])
        eps = pr.sb(c, "n_eps", [P, 1])
        std = pr.sb(c, "n_std", [P, 2, T, 1])
        rstd = pr.sb(c, "n_rstd", [P, 2, T, 1])
        s_in = [pr.counter(f"n_in{i}", 16) for i in range(2)]
        s_st = [pr.counter(f"n_st{i}", 16) for i in range(2)]
        s_eps, s_bn, s_mv, s_sd, s_rs, s_y = [pr.counter(x) for x in ("n_eps", "n_bn", "n_mv", "n_sd", "n_rs", "n_y")]
        block = c.enter_context(nc.Block())

        def view(t, g):
            return t[bass.ds(node_base(pr, g), GROUP), :].rearrange("(t p) f -> p t f", p=P)

        def each(eng, body):
            body(0, 0, 0)
            body(1, 0, 1)
            with eng.Fori(1, G // 2 - 1) as i:
                body(i * 2, i, 0)
                body(i * 2 + 1, i, 1)
            body(G - 2, G // 2 - 1, 0)
            body(G - 1, G // 2 - 1, 1)

        @block.sync
        def _(sp):
            def load(g, i, s):
                if not (isinstance(i, int) and i == 0):
                    sp.wait_ge(s_y.sem, s_y.at(g - 1))
                sp.dma_start(rows[:, s, :, :], view(frm, g)).then_inc(s_in[s].sem, 16)
            each(sp, load)

        @block.scalar
        def _(act):
            act.wait_ge(s_eps.sem, s_eps.at(1))

            def body(g, i, s):
                act.wait_ge(s_mv.sem, s_mv.at(g + 1))
                act.activation(std[:, s, :, 0], mv[:, s, :, 1], ACT.Sqrt, bias=eps[:, :]).then_inc(s_sd.sem, 1)
                act.wait_ge(s_y.sem, s_y.at(g + 1))
                if isinstance(g, int) and g == G - 1:
                    act.wait_ge(s_st[1 - s].sem, s_st[1 - s].at(G // 2))
                act.dma_start(view(to, g), done[:, s, :, :]).then_inc(s_st[s].sem, 16)
            each(act, body)
            for s in range(2):
                act.wait_ge(s_st[s].sem, s_st[s].at(G // 2))

        @block.vector
        def _(v):
            v.memset(eps[:, :], EPS).then_inc(s_eps.sem, 1)

            def body(g, i, s):
                v.wait_ge(s_in[s].sem, s_in[s].at(i + 1))
                for t in range(T):
                    ins = v.bn_stats(stats[:, s, t, :], rows[:, s, t, :])
                ins.then_inc(s_bn.sem, 1)
                v.wait_ge(s_bn.sem, s_bn.at(g + 1))
                v.memset(rstd[:, s, :, 0], 0.0)
                for t in range(T):
                    ins = v.bn_aggr(mv[:, s, t, :], stats[:, s, t, :])
                ins.then_inc(s_mv.sem, 1)
                v.wait_ge(s_sd.sem, s_sd.at(g + 1))
                v.reciprocal(rstd[:, s, :, 0], std[:, s, :, 0]).then_inc(s_rs.sem, 1)
                v.wait_ge(s_rs.sem, s_rs.at(g + 1))
                if not (isinstance(i, int) and i == 0):
                    v.wait_ge(s_st[s].sem, s_st[s].at(i))
                for t in range(T):
                    ins = v.tensor_scalar(done[:, s, t, :], rows[:, s, t, :], mv[:, s, t, 0:1], rstd[:, s, t, :],
                                          ALU.subtract, ALU.mult)
                ins.then_inc(s_y.sem, 1)
            each(v, body)
    for s in range(2):
        s_in[s].passed(G // 2)
        s_st[s].passed(G // 2)
    s_eps.passed(1)
    for q in (s_bn, s_mv, s_sd, s_rs, s_y):
        q.passed(G)


def build(nc, x, src, dst, a_wl1, a_b1, a_wr1, a_wl2, a_b2, a_wr2, b_wl1, b_b1, b_wr1, b_wl2, b_b2, b_wr2,
          b_wl3, b_b3, b_wr3, out):
    N = x.shape[0]

    def scratch(name, width):
        return nc.dram_tensor(name, [N, width], F32, kind="Internal").ap()

    h1, o1, x1 = scratch("h1", 128), scratch("o1", 128), scratch("x1", 128)
    g1, g2, o2 = scratch("g1", 256), scratch("g2", 256), scratch("o2", 128)
    with ExitStack() as ctx:
        pr = Program(nc, ctx, N, src.shape[0])
        convs = [
            dict(name="a1", h=x, out=h1, relu=False, w=1, f_out=128, turned=True, Wl=a_wl1, Wr=a_wr1, b=a_b1),
            dict(name="a2", h=h1, out=o1, relu=True, w=1, f_out=128, turned=True, Wl=a_wl2, Wr=a_wr2, b=a_b2,
                 res=x),
            dict(name="b1", h=x1, out=g1, relu=False, w=1, f_out=256, turned=False, Wl=b_wl1, Wr=b_wr1, b=b_b1),
            dict(name="b2", h=g1, out=g2, relu=True, w=2, f_out=256, turned=False, Wl=b_wl2, Wr=b_wr2, b=b_b2),
            dict(name="b3", h=g2, out=o2, relu=True, w=2, f_out=128, turned=False, Wl=b_wl3, Wr=b_wr3, b=b_b3,
                 res=x1),
        ]
        constants(pr)
        edge_tables(pr, src, dst)
        window_tables(pr)
        weights(pr, convs)
        odd = nc.values_load(pr.odd[0:1, 0:1], min_val=0, max_val=1 << 20,
                             skip_runtime_bounds_check_because="a count of node tiles")
        with nc.If(odd == 0):
            for cv in convs:
                pr.stage = cv["name"]
                fused_pass(pr, dict(cv, out={"a2": x1, "b3": out}.get(cv["name"], cv["out"])))
        with nc.Else():
            for cv in convs:
                pr.stage = "general_" + cv["name"]
                dense_pass(pr, cv)
                edge_pass(pr, cv)
                if cv["name"] == "a2":
                    norm_pass(pr, o1, x1)
                if cv["name"] == "b3":
                    norm_pass(pr, o2, out)


_INS = ["x", "src", "dst", "L0_gnn_W1l", "L0_gnn_b1l", "L0_gnn_W1r", "L0_gnn_W2l", "L0_gnn_b2l", "L0_gnn_W2r",
        "L1_gnn_W1l", "L1_gnn_b1", "L1_gnn_W1r", "L1_gnn_W2l", "L1_gnn_b2", "L1_gnn_W2r", "L1_gnn_W3l",
        "L1_gnn_b3", "L1_gnn_W3r"]


def kernel(**inputs):
    import numpy as _np
    import concourse.bacc as _bacc
    from concourse import mybir as _mybir
    from concourse.bass_utils import run_bass_kernel_spmd as _run

    nc = _bacc.Bacc("TRN2", target_bir_lowering=False, num_devices=1)
    arrays, args = {}, []
    for name in _INS:
        a = _np.ascontiguousarray(inputs[name])
        arrays[f"in_{name}_dram"] = a
        args.append(nc.dram_tensor(f"in_{name}_dram", a.shape, _mybir.dt.from_np(a.dtype), kind="ExternalInput").ap())
    shape = inputs["x"].shape
    args.append(nc.dram_tensor("out_0_dram", shape, F32, kind="ExternalOutput").ap())
    build(nc, *args)
    r = _run(nc, [arrays], core_ids=[0])
    return r.results[0]["out_0_dram"]
```
